# Optimizing a Trainium2 kernel written in Bass

```python
import numpy as np
import jax
import jax.numpy as jnp

def _softmax(x, axis=-1):
    return jax.nn.softmax(x, axis=axis)

def _gelu(x):
    return jax.nn.gelu(x, approximate=True)

def _silu(x):
    return jax.nn.silu(x)

def _sigmoid(x):
    return jax.nn.sigmoid(x)

def _layernorm(x, axis=-1, eps=1e-05):
    m = jnp.mean(x, axis=axis, keepdims=True)
    v = jnp.var(x, axis=axis, keepdims=True)
    return (x - m) / jnp.sqrt(v + eps)

def _scatter_add(tgt, idx, src, axis=0):
    return tgt.at[idx].add(src)

def _segment_sum(src, seg, n):
    return jax.ops.segment_sum(src, seg, n)
kernel_name = 'mk_macaron_d2_jaxref_r8_a78b52'

def setup_inputs(seed: int=0):
    np.random.seed(seed)
    _w = jnp.asarray

    def _L0_attn_setup():
        import jax, jax.numpy as jnp
        import numpy as np
        D_MODEL = 128
        N_HEADS = 16
        D_HEAD = D_MODEL // N_HEADS
        M_SLOPE = 0.5
        BATCH = 2
        SEQ = 256

        def _alibi_bias(n_heads, seq_len, m, dtype):
            slopes = m ** jnp.arange(n_heads, dtype=dtype)
            pos = jnp.arange(seq_len, dtype=dtype)
            dist = jnp.abs(pos[:, None] - pos[None, :])
            return -dist[None, :, :] * slopes[:, None, None]
        key = jax.random.key(seed)
        k1, k2, k3 = jax.random.split(key, 3)
        x = jax.random.normal(k1, (BATCH, SEQ, D_MODEL), dtype=jnp.float32)
        qkv_w = jax.random.normal(k2, (3 * D_MODEL, D_MODEL), dtype=jnp.float32) * (1.0 / np.sqrt(D_MODEL))
        qkv_b = jnp.zeros((3 * D_MODEL,), dtype=jnp.float32)
        out_w = jax.random.normal(k3, (D_MODEL, D_MODEL), dtype=jnp.float32) * (1.0 / np.sqrt(D_MODEL))
        out_b = jnp.zeros((D_MODEL,), dtype=jnp.float32)
        return {'x': x, 'qkv_w': qkv_w, 'qkv_b': qkv_b, 'out_w': out_w, 'out_b': out_b}
    _L0_attn_in = _L0_attn_setup()

    def _L0_ffn_setup():
        import jax, jax.numpy as jnp
        import numpy as np
        DIM = 128
        DEPTH = 2
        HEADS = 8
        DIM_HEAD = 64
        WINDOW = 64
        INNER = HEADS * DIM_HEAD
        HID = int(DIM * 4 * 2 / 3)
        B, N = (2, 1024)
        QK_SCALE = 8.0

        def shift_token(t):
            t1, t2 = jnp.split(t, 2, axis=-1)
            t2 = jnp.pad(t2, ((0, 0), (1, 0), (0, 0)))[:, :-1]
            return jnp.concatenate([t1, t2], axis=-1)

        def l2norm(t):
            return t / jnp.clip(jnp.linalg.norm(t, axis=-1, keepdims=True), 1e-12)

        def rotate_half(x):
            x1, x2 = jnp.split(x, 2, axis=-1)
            return jnp.concatenate([-x2, x1], axis=-1)

        def rotary_xpos(q, k):
            n = q.shape[-2]
            half_idx = jnp.arange(0, DIM_HEAD, 2, dtype=jnp.float32)
            inv_freq = 1.0 / 10000.0 ** (half_idx / DIM_HEAD)
            t = jnp.arange(n, dtype=jnp.float32)
            freqs = t[:, None] * inv_freq[None, :]
            freqs = jnp.concatenate([freqs, freqs], axis=-1)
            base = (half_idx + 0.4 * DIM_HEAD) / (1.4 * DIM_HEAD)
            power = (t - n // 2) / float(WINDOW // 2)
            scale = base[None, :] ** power[:, None]
            scale = jnp.concatenate([scale, scale], axis=-1)
            cos, sin = (jnp.cos(freqs), jnp.sin(freqs))
            q = q * cos * scale + rotate_half(q) * sin * scale
            k = k * cos / scale + rotate_half(k) * sin / scale
            return (q, k)

        def local_attention(q, k, v):
            b, h, n, d = q.shape
            w = n // WINDOW
            bq = q.reshape(b, h, w, WINDOW, d) * QK_SCALE
            bk = k.reshape(b, h, w, WINDOW, d)
            bv = v.reshape(b, h, w, WINDOW, d)

            def look_around(t):
                p = jnp.pad(t, ((0, 0), (0, 0), (1, 0), (0, 0), (0, 0)))
                return jnp.concatenate([p[:, :, :w], p[:, :, 1:]], axis=3)
            bk, bv = (look_around(bk), look_around(bv))
            bt = jnp.arange(n).reshape(w, WINDOW)
            btp = jnp.pad(bt, ((1, 0), (0, 0)), constant_values=-1)
            btk = jnp.concatenate([btp[:w], btp[1:]], axis=1)
            sim = jnp.einsum('bhwid,bhwjd->bhwij', bq, bk)
            i = bt[:, :, None]
            j = btk[:, None, :]
            mask = (i < j) | (i > j + WINDOW) | (j == -1)
            sim = jnp.where(mask, -jnp.finfo(sim.dtype).max, sim)
            attn = jax.nn.softmax(sim, axis=-1)
            out = jnp.einsum('bhwij,bhwjd->bhwid', attn, bv)
            return out.reshape(b, h, n, d)

        def _layer(x, wqkv, qs, ksc, wo, lg, lb, w1, b1, w2, b2):
            b, n, _ = x.shape
            h = shift_token(x)
            qkv = h @ wqkv
            q, k, v = jnp.split(qkv, 3, axis=-1)
            to_heads = lambda t: t.reshape(b, n, HEADS, DIM_HEAD).transpose(0, 2, 1, 3)
            q, k, v = (to_heads(q), to_heads(k), to_heads(v))
            q = l2norm(q) * qs
            k = l2norm(k) * ksc
            q, k = rotary_xpos(q, k)
            o = local_attention(q, k, v)
            o = o.transpose(0, 2, 1, 3).reshape(b, n, INNER)
            x = x + o @ wo
            h = shift_token(x)
            mu = h.mean(-1, keepdims=True)
            var = h.var(-1, keepdims=True)
            h = (h - mu) / jnp.sqrt(var + 1e-05) * lg + lb
            h = h @ w1 + b1
            a, g = jnp.split(h, 2, axis=-1)
            h = a * jax.nn.gelu(g, approximate=False)
            x = x + h @ w2 + b2
            return x
        key = jax.random.key(seed)
        ks = jax.random.split(key, 6)
        return {'x': jax.random.normal(ks[0], (B, N, DIM), jnp.float32), 'wqkv': jax.random.normal(ks[1], (DEPTH, DIM, 3 * INNER), jnp.float32) * 0.02, 'q_scale': jnp.ones((DEPTH, DIM_HEAD), jnp.float32), 'k_scale': jnp.ones((DEPTH, DIM_HEAD), jnp.float32), 'wo': jax.random.normal(ks[2], (DEPTH, INNER, DIM), jnp.float32) * 0.02, 'ln_g': jnp.ones((DEPTH, DIM), jnp.float32), 'ln_b': jnp.zeros((DEPTH, DIM), jnp.float32), 'w1': jax.random.normal(ks[3], (DEPTH, DIM, 2 * HID), jnp.float32) * 0.02, 'b1': jnp.zeros((DEPTH, 2 * HID), jnp.float32), 'w2': jax.random.normal(ks[4], (DEPTH, HID, DIM), jnp.float32) * 0.02, 'b2': jnp.zeros((DEPTH, DIM), jnp.float32)}
    _L0_ffn_in = _L0_ffn_setup()

    def _L1_attn_setup():
        import jax, jax.numpy as jnp
        import numpy as np
        NUM_HEADS = 32
        EPS = 1e-15
        key = jax.random.key(seed)
        k1, k2, k3, k4 = jax.random.split(key, 4)
        B, N, C = (8, 512, 128)
        x = jax.random.normal(k1, (B, N, C), dtype=jnp.float32)
        qkv_weight = jax.random.normal(k2, (3 * C, C), dtype=jnp.float32) * C ** (-0.5)
        proj_weight = jax.random.normal(k3, (C, C), dtype=jnp.float32) * C ** (-0.5)
        proj_bias = jax.random.normal(k4, (C,), dtype=jnp.float32) * 0.01
        return {'x': x, 'qkv_weight': qkv_weight, 'proj_weight': proj_weight, 'proj_bias': proj_bias}
    _L1_attn_in = _L1_attn_setup()

    def _L1_ffn_setup():
        import jax, jax.numpy as jnp
        import numpy as np
        B, S, H, F, E = (4, 256, 128, 512, 8)
        key = jax.random.key(seed)
        ks = jax.random.split(key, 8)
        s = 1.0 / np.sqrt(H)
        sf = 1.0 / np.sqrt(F)
        return {'x': jax.random.normal(ks[0], (B, S, H), jnp.float32), 'wr': jax.random.uniform(ks[1], (H, E), jnp.float32, -s, s), 'br': jax.random.uniform(ks[2], (E,), jnp.float32, -s, s), 'w1': jax.random.uniform(ks[3], (E, H, F), jnp.float32, -s, s), 'b1': jax.random.uniform(ks[4], (E, F), jnp.float32, -s, s), 'w2': jax.random.uniform(ks[5], (E, F, H), jnp.float32, -sf, sf), 'b2': jax.random.uniform(ks[6], (E, H), jnp.float32, -sf, sf)}
    _L1_ffn_in = _L1_ffn_setup()
    _d = {'L0_attn_x': _L0_attn_in['x'], 'L0_attn_qkv_w': _L0_attn_in['qkv_w'], 'L0_attn_qkv_b': _L0_attn_in['qkv_b'], 'L0_attn_out_w': _L0_attn_in['out_w'], 'L0_attn_out_b': _L0_attn_in['out_b'], 'L0_ffn_wqkv': _L0_ffn_in['wqkv'], 'L0_ffn_q_scale': _L0_ffn_in['q_scale'], 'L0_ffn_k_scale': _L0_ffn_in['k_scale'], 'L0_ffn_wo': _L0_ffn_in['wo'], 'L0_ffn_ln_g': _L0_ffn_in['ln_g'], 'L0_ffn_ln_b': _L0_ffn_in['ln_b'], 'L0_ffn_w1': _L0_ffn_in['w1'], 'L0_ffn_b1': _L0_ffn_in['b1'], 'L0_ffn_w2': _L0_ffn_in['w2'], 'L0_ffn_b2': _L0_ffn_in['b2'], 'L1_attn_qkv_weight': _L1_attn_in['qkv_weight'], 'L1_attn_proj_weight': _L1_attn_in['proj_weight'], 'L1_attn_proj_bias': _L1_attn_in['proj_bias'], 'L1_ffn_wr': _L1_ffn_in['wr'], 'L1_ffn_br': _L1_ffn_in['br'], 'L1_ffn_w1': _L1_ffn_in['w1'], 'L1_ffn_b1': _L1_ffn_in['b1'], 'L1_ffn_w2': _L1_ffn_in['w2'], 'L1_ffn_b2': _L1_ffn_in['b2']}
    _x0 = _d['L0_attn_x']
    _d['L0_attn_x'] = jax.random.normal(jax.random.fold_in(jax.random.key(seed), 1), (16, 256, 128), dtype=_x0.dtype)
    del _x0
    return _d

def reference(L0_attn_x, L0_attn_qkv_w, L0_attn_qkv_b, L0_attn_out_w, L0_attn_out_b, L0_ffn_wqkv, L0_ffn_q_scale, L0_ffn_k_scale, L0_ffn_wo, L0_ffn_ln_g, L0_ffn_ln_b, L0_ffn_w1, L0_ffn_b1, L0_ffn_w2, L0_ffn_b2, L1_attn_qkv_weight, L1_attn_proj_weight, L1_attn_proj_bias, L1_ffn_wr, L1_ffn_br, L1_ffn_w1, L1_ffn_b1, L1_ffn_w2, L1_ffn_b2):

    def _L0_attn_ref(x, qkv_w, qkv_b, out_w, out_b):
        import jax, jax.numpy as jnp
        import numpy as np
        D_MODEL = 128
        N_HEADS = 16
        D_HEAD = D_MODEL // N_HEADS
        M_SLOPE = 0.5
        BATCH = 2
        SEQ = 256

        def _alibi_bias(n_heads, seq_len, m, dtype):
            slopes = m ** jnp.arange(n_heads, dtype=dtype)
            pos = jnp.arange(seq_len, dtype=dtype)
            dist = jnp.abs(pos[:, None] - pos[None, :])
            return -dist[None, :, :] * slopes[:, None, None]
        batch, seq_len, d_model = x.shape
        qkv = x @ qkv_w.T + qkv_b
        qkv = qkv.reshape(batch, seq_len, N_HEADS, 3 * D_HEAD).transpose(0, 2, 1, 3)
        q, k, v = jnp.split(qkv, 3, axis=-1)
        scale = jnp.sqrt(jnp.asarray(D_HEAD, dtype=x.dtype))
        scores = jnp.einsum('bhid,bhjd->bhij', q, k) / scale
        scores = scores + _alibi_bias(N_HEADS, seq_len, M_SLOPE, x.dtype)[None]
        attn = jax.nn.softmax(scores, axis=-1)
        out = jnp.einsum('bhij,bhjd->bhid', attn, v)
        out = out.transpose(0, 2, 1, 3).reshape(batch, seq_len, d_model)
        return out @ out_w.T + out_b

    def _L0_ffn_ref(x, wqkv, q_scale, k_scale, wo, ln_g, ln_b, w1, b1, w2, b2):
        import jax, jax.numpy as jnp
        import numpy as np
        DIM = 128
        DEPTH = 2
        HEADS = 8
        DIM_HEAD = 64
        WINDOW = 64
        INNER = HEADS * DIM_HEAD
        HID = int(DIM * 4 * 2 / 3)
        B, N = (2, 1024)
        QK_SCALE = 8.0

        def shift_token(t):
            t1, t2 = jnp.split(t, 2, axis=-1)
            t2 = jnp.pad(t2, ((0, 0), (1, 0), (0, 0)))[:, :-1]
            return jnp.concatenate([t1, t2], axis=-1)

        def l2norm(t):
            return t / jnp.clip(jnp.linalg.norm(t, axis=-1, keepdims=True), 1e-12)

        def rotate_half(x):
            x1, x2 = jnp.split(x, 2, axis=-1)
            return jnp.concatenate([-x2, x1], axis=-1)

        def rotary_xpos(q, k):
            n = q.shape[-2]
            half_idx = jnp.arange(0, DIM_HEAD, 2, dtype=jnp.float32)
            inv_freq = 1.0 / 10000.0 ** (half_idx / DIM_HEAD)
            t = jnp.arange(n, dtype=jnp.float32)
            freqs = t[:, None] * inv_freq[None, :]
            freqs = jnp.concatenate([freqs, freqs], axis=-1)
            base = (half_idx + 0.4 * DIM_HEAD) / (1.4 * DIM_HEAD)
            power = (t - n // 2) / float(WINDOW // 2)
            scale = base[None, :] ** power[:, None]
            scale = jnp.concatenate([scale, scale], axis=-1)
            cos, sin = (jnp.cos(freqs), jnp.sin(freqs))
            q = q * cos * scale + rotate_half(q) * sin * scale
            k = k * cos / scale + rotate_half(k) * sin / scale
            return (q, k)

        def local_attention(q, k, v):
            b, h, n, d = q.shape
            w = n // WINDOW
            bq = q.reshape(b, h, w, WINDOW, d) * QK_SCALE
            bk = k.reshape(b, h, w, WINDOW, d)
            bv = v.reshape(b, h, w, WINDOW, d)

            def look_around(t):
                p = jnp.pad(t, ((0, 0), (0, 0), (1, 0), (0, 0), (0, 0)))
                return jnp.concatenate([p[:, :, :w], p[:, :, 1:]], axis=3)
            bk, bv = (look_around(bk), look_around(bv))
            bt = jnp.arange(n).reshape(w, WINDOW)
            btp = jnp.pad(bt, ((1, 0), (0, 0)), constant_values=-1)
            btk = jnp.concatenate([btp[:w], btp[1:]], axis=1)
            sim = jnp.einsum('bhwid,bhwjd->bhwij', bq, bk)
            i = bt[:, :, None]
            j = btk[:, None, :]
            mask = (i < j) | (i > j + WINDOW) | (j == -1)
            sim = jnp.where(mask, -jnp.finfo(sim.dtype).max, sim)
            attn = jax.nn.softmax(sim, axis=-1)
            out = jnp.einsum('bhwij,bhwjd->bhwid', attn, bv)
            return out.reshape(b, h, n, d)

        def _layer(x, wqkv, qs, ksc, wo, lg, lb, w1, b1, w2, b2):
            b, n, _ = x.shape
            h = shift_token(x)
            qkv = h @ wqkv
            q, k, v = jnp.split(qkv, 3, axis=-1)
            to_heads = lambda t: t.reshape(b, n, HEADS, DIM_HEAD).transpose(0, 2, 1, 3)
            q, k, v = (to_heads(q), to_heads(k), to_heads(v))
            q = l2norm(q) * qs
            k = l2norm(k) * ksc
            q, k = rotary_xpos(q, k)
            o = local_attention(q, k, v)
            o = o.transpose(0, 2, 1, 3).reshape(b, n, INNER)
            x = x + o @ wo
            h = shift_token(x)
            mu = h.mean(-1, keepdims=True)
            var = h.var(-1, keepdims=True)
            h = (h - mu) / jnp.sqrt(var + 1e-05) * lg + lb
            h = h @ w1 + b1
            a, g = jnp.split(h, 2, axis=-1)
            h = a * jax.nn.gelu(g, approximate=False)
            x = x + h @ w2 + b2
            return x
        for l in range(DEPTH):
            x = _layer(x, wqkv[l], q_scale[l], k_scale[l], wo[l], ln_g[l], ln_b[l], w1[l], b1[l], w2[l], b2[l])
        return x

    def _L1_attn_ref(x, qkv_weight, proj_weight, proj_bias):
        import jax, jax.numpy as jnp
        import numpy as np
        NUM_HEADS = 32
        EPS = 1e-15
        B, N, C = x.shape
        H = NUM_HEADS
        D = C // H
        qkv = jax.nn.relu(jnp.einsum('bnc,oc->bno', x, qkv_weight))
        qkv = qkv.reshape(B, N, 3, H, D)
        q, k, v = (qkv[:, :, 0], qkv[:, :, 1], qkv[:, :, 2])
        v_pad = jnp.concatenate([v, jnp.ones((B, N, H, 1), dtype=v.dtype)], axis=-1)
        vk = jnp.einsum('bnhe,bnhd->bhed', v_pad.astype(jnp.float32), k.astype(jnp.float32))
        vk_q = jnp.einsum('bhed,bnhd->bnhe', vk, q.astype(jnp.float32))
        proj_input = (vk_q[..., :D] / (vk_q[..., D:] + EPS)).astype(qkv.dtype)
        proj_input = proj_input.reshape(B, N, C)
        y = jnp.einsum('bnc,oc->bno', proj_input, proj_weight) + proj_bias
        return y

    def _L1_ffn_ref(x, wr, br, w1, b1, w2, b2):
        import jax, jax.numpy as jnp
        import numpy as np
        B, S, H, F, E = (4, 256, 128, 512, 8)
        scores = jnp.einsum('bsh,he->bse', x, wr) + br
        expert_id = jnp.argmax(scores, axis=-1)
        h = jnp.einsum('bsh,ehf->ebsf', x, w1) + b1[:, None, None, :]
        h = jax.nn.gelu(h, approximate=False)
        y = jnp.einsum('ebsf,efh->ebsh', h, w2) + b2[:, None, None, :]
        one_hot = jax.nn.one_hot(expert_id, E, dtype=x.dtype)
        out = jnp.einsum('ebsh,bse->bsh', y, one_hot)
        return out
    x = L0_attn_x
    x = x + 0.5 * _L0_ffn_ref(_layernorm(x, axis=-1), L0_ffn_wqkv, L0_ffn_q_scale, L0_ffn_k_scale, L0_ffn_wo, L0_ffn_ln_g, L0_ffn_ln_b, L0_ffn_w1, L0_ffn_b1, L0_ffn_w2, L0_ffn_b2)
    x = x + _L0_attn_ref(_layernorm(x, axis=-1), L0_attn_qkv_w, L0_attn_qkv_b, L0_attn_out_w, L0_attn_out_b)
    x = x + 0.5 * _L0_ffn_ref(_layernorm(x, axis=-1), L0_ffn_wqkv, L0_ffn_q_scale, L0_ffn_k_scale, L0_ffn_wo, L0_ffn_ln_g, L0_ffn_ln_b, L0_ffn_w1, L0_ffn_b1, L0_ffn_w2, L0_ffn_b2)
    x = x + 0.5 * _L1_ffn_ref(_layernorm(x, axis=-1), L1_ffn_wr, L1_ffn_br, L1_ffn_w1, L1_ffn_b1, L1_ffn_w2, L1_ffn_b2)
    x = x + _L1_attn_ref(_layernorm(x, axis=-1), L1_attn_qkv_weight, L1_attn_proj_weight, L1_attn_proj_bias)
    x = x + 0.5 * _L1_ffn_ref(_layernorm(x, axis=-1), L1_ffn_wr, L1_ffn_br, L1_ffn_w1, L1_ffn_b1, L1_ffn_w2, L1_ffn_b2)
    return x

_drawn_inputs = setup_inputs


def setup_inputs(seed=0):
    import zlib

    import numpy as np

    out = dict(_drawn_inputs(seed))
    spreads = {'L0_attn_qkv_b': (0.0, 0.1),
     'L0_attn_out_b': (0.0, 0.1),
     'L0_ffn_q_scale': (1.0, 0.6),
     'L0_ffn_k_scale': (1.0, 0.6),
     'L0_ffn_ln_g': (1.0, 0.6),
     'L0_ffn_ln_b': (0.0, 0.8),
     'L0_ffn_b1': (0.0, 0.682),
     'L0_ffn_b2': (0.0, 0.1)}
    factors = {'L0_ffn_w1': 3.806,
     'L0_ffn_w2': 3.837,
     'L1_attn_proj_bias': 8.0,
     'L1_ffn_b1': 5.476,
     'L1_ffn_b2': 4.092,
     'L1_ffn_br': 3.684}
    for name, (base, spread) in spreads.items():
        noise = np.random.default_rng([zlib.crc32(name.encode()), seed]).standard_normal(out[name].shape)
        drawn = base * np.exp(spread * noise) if base else spread * noise
        out[name] = jnp.asarray(drawn.astype(out[name].dtype))
    for name, factor in factors.items():
        out[name] = (out[name] * factor).astype(out[name].dtype)
    return out
```

```python
from contextlib import ExitStack

import numpy as np

import concourse.bass as bass
from concourse import mybir

F32 = mybir.dt.float32
F32R = mybir.dt.float32r
BF16 = mybir.dt.bfloat16
ALU = mybir.AluOpType
ACT = mybir.ActivationFunctionType
AX = mybir.AxisListType.X

SEQS, T, D = 16, 256, 128
LANES = 2
TURNS = SEQS // LANES
TILES = T // 128
P = 128
HEADS, DH, WIN = 8, 64, 64
INNER = HEADS * DH
HID = int(D * 4 * 2 / 3)
HC = 3
DEPTH = 2
QK_SCALE = 8.0
ST_HEADS = ((0, 2), (1, 3), (0, 2, 4, 6), (4, 6), (5, 7), (1, 3, 5, 7))
J0W, J1W = 192, 128
JW = J0W + J1W
AH, ADH = 16, 8
SLOT = 32
O_TILE = (AH - 1) * (ADH + 1) + P
ROW_POS, ROW_ONE, ROW_MHI, ROW_MLO = 24, 25, 26, 27
NE, EF = 8, 512
EC = EF // P
LH = 32
LDH = D // LH
EPS = 1e-5
MASKED = -1e30
LN_SET = "natural_log_exp_and_others"

LN_RATE = dict(x_in=1, mean_ready=1, centered=1, squared=1, var_ready=1, log_var=1, rstd=1, normed=1)
LAYER_RATE = dict(
    h_hi=2, h_lo=2, qk_ready=1, qk_sb=1, v_ready=1, v_sb=1, sq_sb=1, ss=1, ss_max=1, ln_ss=1, rnorm=1,
    t_cos=1, t_sin=1, t_sum=1, qk_rot=1, qkT_ready=1, qT_sb=1, kT_sb=1, q_bf=1, k_bf=1, s_ready=3, s_max=3,
    m_hi=1, m_lo=1, mT_ready=1, mT_sb=1, st_ready=6, p_sb=6, o_ready=1, o_rec=1, o_sb=1, oT_ready=1,
    oT_hi=1, oT_lo=1, proj_ready=1, resid=1, up_ready=1, gelu_sb=1, u_sb=1, u_hi=1, u_lo=1, down_ready=1,
    resid2=1)


def ffn_rates():
    r = {k: v * DEPTH for k, v in LAYER_RATE.items()}
    for k, v in LN_RATE.items():
        r[k] = v * (1 + DEPTH)
    r["x_in"] = 1
    r["x_out"] = 1
    return r


ATTN_RATE = LN_RATE | dict(
    h_hi=1, h_lo=1, qk_ready=1, t_cos=2, qT_sb=2, qk_rot=2, v_ready=1, v_sb=1, s_ready=4, s_max=4, m_hi=1, m_lo=1,
    mT_ready=1, mT_sb=1, st_ready=AH, p_sb=AH, o_ready=AH, o_rec=1, o_sb=1, oT_ready=1, oT_hi=1, oT_lo=1,
    proj_ready=1, x_out=1)
MOE_RATE = LN_RATE | dict(
    h_hi=1, h_lo=1, qk_ready=1, ss=1, ss_max=1, t_cos=1, t_sin=1, t_sum=1, qk_rot=1, qkT_ready=1, mT_sb=1,
    mT_ready=1, up_ready=NE, gelu_sb=NE, u_hi=NE, u_lo=NE, down_ready=NE, u_sb=NE + 1, oT_ready=1, x_out=1)
LIN_RATE = LN_RATE | dict(
    h_hi=1, h_lo=1, qk_ready=1, v_ready=1, qT_sb=1, v_sb=1, s_ready=1, m_hi=1, m_lo=1, o_ready=1,
    t_sum=1, o_rec=1, o_sb=1, oT_hi=1, oT_lo=1, proj_ready=1, x_out=1)
PHASES = [("ffn", ffn_rates()), ("attn", ATTN_RATE), ("ffn", ffn_rates()),
          ("moe", MOE_RATE), ("lin", LIN_RATE), ("moe", MOE_RATE)]


def shape_constants():
    t = np.arange(T, dtype=np.float32)
    half = np.arange(0, DH, 2, dtype=np.float32)
    inv = np.float32(1.0) / np.float32(10000.0) ** (half / np.float32(DH))
    fr = t[:, None] * inv[None, :]
    fr = np.concatenate([fr, fr], -1)
    base = (half + np.float32(0.4 * DH)) / np.float32(1.4 * DH)
    power = (t - T // 2) / np.float32(WIN // 2)
    sc = base[None, :] ** power[:, None]
    sc = np.concatenate([sc, sc], -1)
    sign = np.concatenate([-np.ones(DH // 2), np.ones(DH // 2)]).astype(np.float32)
    cos, sin = np.cos(fr), np.sin(fr) * sign
    rot = np.stack([np.stack([cos * sc, sin * sc], 1) * np.float32(QK_SCALE), np.stack([cos / sc, sin / sc], 1)], 1)
    rot = rot.reshape(TILES, P, 2, 2, DH).transpose(1, 0, 2, 3, 4).reshape(P, -1)
    p, f = np.arange(P)[:, None], np.arange(P)[None, :]
    band = lambda i, j: np.where((i < j) | (i > j + WIN), MASKED, 0.0)
    i0, j64 = np.arange(J0W)[None, :], np.arange(WIN, T)[None, :]
    st0, st1 = band(i0, p), band(f + P, p + P)
    s0, s1 = band(p, f), band(p + P, j64)
    eye = np.eye(P)
    sel = np.zeros((P, HEADS, P))
    for h in range(HEADS):
        sel[h, h] = sel[h + HEADS, h] = 1.0
    relu_pf, relu_fp = np.maximum(p - f, 0), np.maximum(f - p, 0)
    pos = np.arange(T)
    slopes = 0.5 ** np.arange(AH)
    qc, kc = np.zeros((P, T)), np.zeros((P, AH // 4, T))
    lo_q, lo_k = np.zeros((P, 1)), np.zeros((P, 1))
    sgn = np.where(pos < P, 1.0, -1.0)
    for s in range(4):
        r = s * SLOT
        qc[r + ROW_POS], qc[r + ROW_ONE] = pos, 1.0
        for c in range(AH // 4):
            m = slopes[4 * c + s]
            kc[r + ROW_POS, c] = -sgn * m
            kc[r + ROW_ONE, c] = sgn * m * pos
            kc[r + ROW_MHI, c] = kc[r + ROW_MLO, c] = 1.0
        lo_q[r + 8:r + 16] = -1.0
        lo_k[r + 16:r + 24] = -1.0
    slope_eye = np.concatenate([-2.0 * m * eye for m in slopes], 1)
    block = (p // LDH == f // LDH).astype(np.float32)
    order = np.tile(np.arange(NE, 0, -1), (P, TILES))
    parts = dict(rot=rot, masks=np.concatenate([st0, st1, s0, s1], 1), relu=np.concatenate([relu_pf, relu_fp], 1),
                 qc=qc, sel=sel.reshape(P, -1), slope_eye=slope_eye,
                 eye=eye, kc=kc.reshape(P, -1), lo_q=lo_q, lo_k=lo_k, block=block, order=order,
                 parity=np.stack([np.arange(P) < DH, np.arange(P) >= DH], 1))
    at, n = {}, 0
    for k, v in parts.items():
        at[k] = (n, n + v.shape[1])
        n += v.shape[1]
    return np.concatenate([v.astype(np.float32) for v in parts.values()], 1), at


def build(nc, io, at):
    ctx = ExitStack()
    with ctx:
        def sb(name, shape, dt=F32, on=ctx):
            return on.enter_context(nc.sbuf_tensor(name, shape, dt))

        def sem(name):
            return ctx.enter_context(nc.semaphore(name))

        lanes = range(LANES)
        R = [ctx.enter_context(nc.psum_tensor(f"psum{L}", [P, 4, 512], F32)) for L in lanes]
        X = sb("x_all", [P, SEQS, T])
        Xl = [sb(f"x{L}", [P, T]) for L in lanes]
        Y = [sb(f"y{L}", [P, T + 1]) for L in lanes]
        cen = [sb(f"centered{L}", [P, T]) for L in lanes]
        sqr = [sb(f"squared{L}", [P, T]) for L in lanes]
        lnv = rst = sqr
        sqs = sb("qk_squares", [P, 2048])
        work = [sb(f"work{L}", [P, 6144]) for L in lanes]
        A = [w[:, 0:2048] for w in work]
        B = [w[:, 2048:4096] for w in work]
        C = [w[:, 4096:6144] for w in work]
        sm = [sb(f"small{L}", [P, 256]) for L in lanes]
        mneg = [sb(f"m_neg{L}", [P, TILES, 2 * HEADS], BF16) for L in lanes]
        mT = [sb(f"mT{L}", [P, T], BF16) for L in lanes]
        qkT = [a.rearrange("p (g c t) -> p g c t", g=2, c=4) for a in A]
        PT = [w[:, 2048:2048 + HEADS * JW].rearrange("p (h i) -> p h i", h=HEADS) for w in work]
        q_par = [(w[:, 0:1024].rearrange("p (c t) -> p c t", c=4), w[:, 4608:5632].rearrange("p (c t) -> p c t", c=4))
                 for w in work]
        O = [w[:, 0:TILES * INNER] for w in work]
        U = [w[:, 2048:2048 + HC * T].rearrange("p (c t) -> p c t", c=HC) for w in work]
        G = [w[:, 2816:2816 + HC * T].rearrange("p (c t) -> p c t", c=HC) for w in work]

        ones = sb("mean_weights", [P, P])
        one_col = sb("one_col", [P, 2])
        eps = sb("eps", [P, 1])
        half_ln = sb("half_ln", [P, 1])
        eye = sb("eye", [P, P])
        eyeb = sb("eye_bf", [P, P], BF16)
        masks = sb("masks_bf", [P, 2 * JW], BF16)
        mst0, mst1 = masks[:, 0:J0W], masks[:, J0W:JW]
        ms0, ms1 = masks[:, JW:JW + P], masks[:, JW + P:2 * JW]
        sel = sb("m_rows_bf", [P, HEADS, P], BF16)
        parity = sb("parity", [P, 2])
        tab = sb("rot_tables", [P, DEPTH, 2, TILES, 2, DH])
        relub = sb("relu_bf", [P, 2, P], BF16)
        slopeb = sb("slope_eye_bf", [P, AH, P], BF16)
        lo_q, lo_k = sb("lo_q", [P, 1]), sb("lo_k", [P, 1])
        Tq, Tk = sb("q_rows", [P, 4, T]), sb("k_rows", [P, 4, T])
        block = sb("block", [P, P])
        order = sb("order", [P, TILES, NE])
        bq, bk = sb("bias_q", [P, 4]), sb("bias_k", [P, 4])
        bv = sb("bias_v", [P, D])
        ab = sb("attn_out_bias", [P, 1])
        lb_ = sb("lin_out_bias", [P, 1])
        lnb = sb("ln_b", [P, DEPTH])
        lng = sb("ln_g", [P, DEPTH])
        b1 = sb("b1", [P, DEPTH, 2 * HC])
        b2 = sb("b2", [P, DEPTH])
        wr = sb("router", [P, NE])
        br = sb("router_bias", [P, TILES, NE])
        eb1 = sb("expert_b1", [P, NE, EC])
        eb2 = sb("expert_b2", [NE, D])

        AW = 4 * P * 2 + 2 * P
        LW = 4 * P
        FW = 3 * INNER + 4 * P + 2 * HC * P + HC * P
        aw_hi, aw_lo = sb("attn_w_hi", [P, AW], F32R), sb("attn_w_lo", [P, AW], F32R)
        N_STAGE = at["slope_eye"][1]
        with ExitStack() as early:
            stage = sb("stage", [P, N_STAGE], on=early)
            scl = sb("scales", [P, DEPTH, 2, 2, DH], on=early)
            raw_small = sb("raw_small", [P, AW], on=early)
        hh = [sb(f"h_hi{L}", [P, T], F32R) for L in lanes]
        hl = [sb(f"h_lo{L}", [P, T], F32R) for L in lanes]
        oh = [sb(f"o_hi{L}", [P, 4, T], F32R) for L in lanes]
        ol = [sb(f"o_lo{L}", [P, 4, T], F32R) for L in lanes]
        with ExitStack() as ffn_only:
            qkb = [sb(f"qkT_bf{L}", [P, 3, 4, T], BF16, ffn_only) for L in lanes]
            mpad = [q[:, 0, :, :].rearrange("p c t -> p (c t)").rearrange("p (t h r) -> p t h r", t=TILES, h=AH)
                    for q in qkb]
            Vw = [sb(f"v{L}", [P, TILES * HEADS * (DH + 1) + P], F32, ffn_only) for L in lanes]
            V = [w[:, 0:TILES * HEADS * (DH + 1)].rearrange("p (t h d) -> p t h d", t=TILES, h=HEADS) for w in Vw]
            fw_hi = sb("ffn_w_hi", [P, DEPTH, FW], F32R, ffn_only)
            fw_lo = sb("ffn_w_lo", [P, DEPTH, FW], F32R, ffn_only)
        ew_hi = sb("expert_w_hi", [P, 2, NE, EF], F32R)
        ew_lo = sb("expert_w_lo", [P, 2, NE, EF], F32R)
        lw_hi, lw_lo = sb("lin_w_hi", [P, LW], F32R), sb("lin_w_lo", [P, LW], F32R)
        o1, o2, o3 = 3 * INNER, 3 * INNER + 4 * P, 3 * INNER + 4 * P + 2 * HC * P

        xin = work[0][:, 0:4096].rearrange("p (n d) -> p n d", d=D)
        raw_qkv = work[1][:, 0:2 * o1].rearrange("p (l n) -> p l n", l=2)
        raw_rest = [work[0][:, 4096:4096 + FW - o1], work[1][:, 2 * o1:2 * o1 + FW - o1]]
        raw_lin = work[0][:, NE * EF:NE * EF + LW]
        part = lambda name: stage[:, at[name][0]:at[name][1]]
        raw_e = [work[L][:, 0:NE * EF].rearrange("p (e f) -> p e f", e=NE) for L in lanes]

        S = {name: [sem(f"{name}{L}") for L in lanes] for name in sorted(set().union(*[r for _, r in PHASES]))}
        x_loaded, w_loaded, small_loaded, c_loaded = sem("x_loaded"), sem("w_loaded"), sem("small_loaded"), sem("c_loaded")
        pads, ready, xT_ready, xT_sb = sem("pads"), sem("ready"), sem("xT_ready"), sem("xT_sb")
        lbw, fold, chain = sem("lbw"), sem("fold"), sem("chain")
        ew_loaded, ew_split = sem("ew_loaded"), sem("ew_split")
        xo_ready, xo_sb, stored = sem("xo_ready"), sem("xo_sb"), sem("stored")

        def counter(ph, turn):
            base = {n: sum(r.get(n, 0) for _, r in PHASES[:ph]) * TURNS for n in S}
            base["x_out"] += 1
            rate = PHASES[ph][1]

            def value(name, k=1):
                return turn * rate[name] + (base[name] + k)
            return value

        def st_task(L, k):
            hs = ST_HEADS[k]
            lo, hi, w = (J0W, JW, J1W) if len(hs) == 4 else (0, J0W, J0W)
            return (PT[L][:, hs[0]:hs[-1] + 1:2, lo:hi],
                    R[L][:, k % 4, 0:len(hs) * w].rearrange("p (h i) -> p h i", h=len(hs)))

        def APT(L, t):
            return C[L][:, (t % 4) * 512:(t % 4 + 1) * 512]

        def AV(L):
            return Vw[L][:, 0:TILES * AH * (ADH + 1)]\
                .rearrange("p (t h d) -> p t h d", t=TILES, h=AH)

        def EG(L):
            return A[L][:, 0:EC * T].rearrange("p (c t) -> p c t", c=EC)

        block_ = ctx.enter_context(nc.Block())

        N_C = 8 + 12
        N_SMALL = 26

        @block_.sync
        def _(sp):
            x_t = io["x"].rearrange("b (n p) d -> p (b n) d", p=P)
            for q in range(4):
                sp.dma_start(xin[:, 8 * q:8 * q + 8, :], x_t[:, 8 * q:8 * q + 8, :]).then_inc(x_loaded, 16)
            sp.wait_ge(pads, 3)
            for l in range(DEPTH):
                sp.dma_start(raw_qkv[:, l, :], io["wqkv"][l]).then_inc(w_loaded, 16)
                r = raw_rest[l]
                sp.dma_start(r[:, 0:4 * P].rearrange("p (c n) -> p c n", c=4),
                             io["wo"][l].rearrange("(c p) n -> p c n", p=P)).then_inc(w_loaded, 16)
                for g in range(2):
                    a = o2 - o1 + g * HC * P
                    sp.dma_start(r[:, a:a + HID], io["w1"][l][:, g * HID:(g + 1) * HID]).then_inc(w_loaded, 16)
                for c in range(HC):
                    n = min(P, HID - c * P)
                    a = o3 - o1 + c * P
                    sp.dma_start(r[0:n, a:a + P], io["w2"][l][c * P:c * P + n, :]).then_inc(w_loaded, 16)
            for L in lanes:
                v = counter(3, 0)
                sp.wait_ge(S["x_out"][L], v("x_out", 0))
            sp.dma_start(raw_e[0], io["ew1"].rearrange("e h f -> h e f")).then_inc(ew_loaded, 16)
            sp.dma_start(raw_e[1].rearrange("p e (c n) -> p e c n", c=EC),
                         io["ew2"].rearrange("e (c p) n -> p e c n", p=P)).then_inc(ew_loaded, 16)
            sp.dma_start(raw_lin, io["lin_w"]).then_inc(ew_loaded, 16)
            out_t = io["out"].rearrange("b (n p) d -> p (b n) d", p=P)
            for q in range(8):
                sp.wait_ge(xo_sb, q + 1)
                sp.dma_start(out_t[:, 4 * q:4 * q + 4, :], xin[:, 4 * q:4 * q + 4, :]).then_inc(stored, 16)
            sp.wait_ge(stored, 16 * 8)

        def load_small(eng):
            n = 0

            def load(dst, src):
                nonlocal n
                n += 1
                eng.dma_start(dst, src, allow_slow_non_contiguous=True).then_inc(small_loaded, 16)

            load(raw_small[:, :], io["attn_w"])
            load(bq[:, :], io["bias_q"])
            load(bk[:, :], io["bias_k"])
            load(bv[:, :], io["bias_v"].partition_broadcast(P))
            load(ab[:, :], io["attn_out_b"].rearrange("(p a) -> p a", a=1))
            load(lb_[:, :], io["proj_b"].rearrange("(p a) -> p a", a=1))
            load(lnb[:, :], io["ln_b"].rearrange("l p -> p l"))
            load(lng[:, :], io["ln_g"].rearrange("l p -> p l"))
            load(b2[:, :], io["b2"].rearrange("l p -> p l"))
            for l in range(DEPTH):
                for g in range(2):
                    for c in range(HC):
                        m = min(P, HID - c * P)
                        load(b1[0:m, l, g * HC + c:g * HC + c + 1],
                             io["b1"][l, g * HID + c * P:g * HID + c * P + m].rearrange("(p a) -> p a", a=1))
            load(wr[:, :], io["wr"])
            load(br[:, 0, :], io["br"].partition_broadcast(P))
            load(br[:, 1, :], io["br"].partition_broadcast(P))
            load(eb1[:, :, :], io["eb1"].rearrange("e (c p) -> p e c", p=P))
            load(eb2[:, :], io["eb2"])
            assert n == N_SMALL, n

        def const(name):
            return io["consts"][:, at[name][0]:at[name][1]]

        @block_.gpsimd
        def _(pool):
            for l in range(DEPTH):
                pool.memset(raw_rest[l], 0.0).then_inc(pads, 1)
            pool.memset(b1[:, :, :], 0.0).then_inc(pads, 1)
            pool.wait_ge(pads, 3)
            load_small(pool)
            pool.memset(ones[:, :], 1.0 / D).then_inc(ready, 1)
            pool.memset(one_col[:, :], 1.0).then_inc(ready, 1)
            pool.memset(eps[:, :], EPS).then_inc(ready, 1)
            pool.memset(half_ln[:, :], float(8.0 * np.log(2.0))).then_inc(ready, 1)
            for L in lanes:
                pool.memset(Y[L][:, :], 0.0).then_inc(S["x_out"][L], 1)
                pool.memset(Vw[L][:, :], 1.0).then_inc(ready, 1)

            def ffn(ph):
                with pool.Fori(0, TURNS) as turn:
                    v = counter(ph, turn)
                    for l in range(DEPTH):
                        for L in lanes:
                            a = A[L].rearrange("p (g h d) -> p g h d", g=4, h=HEADS)
                            b = B[L].rearrange("p (g h d) -> p g h d", g=4, h=HEADS)
                            t = tab[:, l, 1, :, :, :].rearrange("p a b d -> p (a b) d")
                            pool.wait_ge(S["qk_sb"][L], v("qk_sb", l + 1))
                            for g in range(4):
                                for s in range(2):
                                    o_, i_ = slice(32 * s, 32 * s + 32), slice(32 - 32 * s, 64 - 32 * s)
                                    last = pool.tensor_tensor(
                                        b[:, g, :, o_], a[:, g, :, i_],
                                        t[:, g, o_].unsqueeze(1).to_broadcast([P, HEADS, 32]), ALU.mult)
                            last.then_inc(S["t_sin"][L], 1)
            ffn(0)
            ffn(2)

        @block_.scalar
        def _(act):
            def ln_stages(v, k, L, src_free=None):
                act.wait_ge(S["centered"][L], v("centered", k))
                act.activation(sqr[L][:, :], cen[L][:, :], ACT.Square).then_inc(S["squared"][L], 1)

            def ln_rstd(v, k, L, bank=3):
                act.wait_ge(S["var_ready"][L], v("var_ready", k))
                act.activation(lnv[L][:, :], R[L][:, bank, T:2 * T], ACT.Ln, bias=eps[:, 0:1])\
                    .then_inc(S["log_var"][L], 1)
                act.wait_ge(S["log_var"][L], v("log_var", k))
                act.activation(rst[L][:, :], lnv[L][:, :], ACT.Exp, scale=-0.5).then_inc(S["rstd"][L], 1)

            def layer_norm(v, k):
                for L in lanes:
                    ln_stages(v, k, L)
                for L in lanes:
                    ln_rstd(v, k, L)

            def ffn(ph):
                with act.Fori(0, TURNS) as turn:
                    v = counter(ph, turn)
                    act.preload_act_table_set(LN_SET)
                    layer_norm(v, 1)
                    for l in range(DEPTH):
                        for L in lanes:
                            act.wait_ge(S["qk_ready"][L], v("qk_ready", l + 1))
                            act.activation(A[L], R[L][:, :, :].rearrange("p b n -> p (b n)"), ACT.Copy)\
                                .then_inc(S["qk_sb"][L], 1)
                            act.wait_ge(S["qk_sb"][L], v("qk_sb", l + 1))
                            if L:
                                act.wait_ge(S["ss"][0], v("ss", l + 1))
                            act.activation(sqs[:, :], A[L], ACT.Square).then_inc(S["sq_sb"][L], 1)
                        for L in lanes:
                            act.wait_ge(S["v_ready"][L], v("v_ready", l + 1))
                            act.activation(V[L][:, :, :, 0:DH],
                                           R[L][:, 0:2, :].rearrange("p t (h d) -> p t h d", h=HEADS), ACT.Copy)\
                                .then_inc(S["v_sb"][L], 1)
                            act.wait_ge(S["ss_max"][L], v("ss_max", l + 1))
                            act.activation(sm[L][:, 64:96], sm[L][:, 32:64], ACT.Ln, scale=65536.0)\
                                .then_inc(S["ln_ss"][L], 1)
                            act.wait_ge(S["ln_ss"][L], v("ln_ss", l + 1))
                            act.activation(sm[L][:, 96:128], sm[L][:, 64:96], ACT.Exp, scale=-0.5,
                                           bias=half_ln[:, 0:1]).then_inc(S["rnorm"][L], 1)
                        for L in lanes:
                            act.wait_ge(S["qkT_ready"][L], v("qkT_ready", l + 1))
                            for g in range(2):
                                last = act.activation(q_par[L][g].rearrange("p c t -> p (c t)"),
                                                      R[L][:, 2:4, :].rearrange("p b n -> p (b n)"), ACT.Copy,
                                                      scale=parity[:, g:g + 1])
                            last.then_inc(S["qT_sb"][L], 1)
                        for L in lanes:
                            for k in range(6):
                                act.wait_ge(S["st_ready"][L], v("st_ready", 6 * l + k + 1))
                                dst, src = st_task(L, k)
                                act.activation(dst, src, ACT.Exp).then_inc(S["p_sb"][L], 1)
                        for L in lanes:
                            act.wait_ge(S["oT_ready"][L], v("oT_ready", l + 1))
                            act.activation(oh[L][:, :, :].rearrange("p c t -> p (c t)"),
                                           R[L][:, 0:2, :].rearrange("p b n -> p (b n)"), ACT.Copy)\
                                .then_inc(S["oT_hi"][L], 1)
                        layer_norm(v, 2 + l)
                        for L in lanes:
                            act.wait_ge(S["up_ready"][L], v("up_ready", l + 1))
                            for c in range(HC):
                                last = act.activation(G[L][:, c, :], R[L][:, 2 + c // 2, (c % 2) * T:(c % 2 + 1) * T],
                                                      ACT.Gelu, bias=b1[:, l, HC + c:HC + c + 1])
                            last.then_inc(S["gelu_sb"][L], 1)
                        act.preload_act_table_set(LN_SET)

            def attn(ph):
                with act.Fori(0, TURNS) as turn:
                    v = counter(ph, turn)
                    layer_norm(v, 1)
                    for L in lanes:
                        for g, src in ((0, A), (1, B)):
                            act.wait_ge(S["t_cos"][L], v("t_cos", g + 1))
                            act.activation(ol[L][:, :, :].rearrange("p c t -> p (c t)") if g == 0 else
                                           oh[L][:, :, :].rearrange("p c t -> p (c t)"),
                                           src[L][:, 0:1024], ACT.Copy).then_inc(S["qT_sb"][L], 1)
                    for t in range(AH):
                        for L in lanes:
                            act.wait_ge(S["st_ready"][L], v("st_ready", t + 1))
                            if t >= 4:
                                act.wait_ge(S["o_ready"][L], v("o_ready", t - 3))
                            act.activation(APT(L, t), R[L][:, t % 3, :], ACT.Exp).then_inc(S["p_sb"][L], 1)
                    for L in lanes:
                        act.wait_ge(S["oT_ready"][L], v("oT_ready", 1))
                        act.activation(hh[L][:, :], R[L][:, 0, 0:T], ACT.Copy).then_inc(S["oT_hi"][L], 1)

            def moe(ph):
                with act.Fori(0, TURNS) as turn:
                    v = counter(ph, turn)
                    act.preload_act_table_set(LN_SET)
                    layer_norm(v, 1)
                    for e in range(NE):
                        for L in lanes:
                            act.wait_ge(S["up_ready"][L], v("up_ready", e + 1))
                            if e:
                                act.wait_ge(S["u_lo"][L], v("u_lo", e))
                            for c in range(EC):
                                last = act.activation(EG(L)[:, c, :], R[L][:, c // 2, (c % 2) * T:(c % 2 + 1) * T],
                                                      ACT.Gelu, bias=eb1[:, e, c:c + 1])
                            last.then_inc(S["gelu_sb"][L], 1)

            def lin(ph):
                with act.Fori(0, TURNS) as turn:
                    v = counter(ph, turn)
                    act.preload_act_table_set(LN_SET)
                    layer_norm(v, 1)
                    for L in lanes:
                        act.wait_ge(S["qk_ready"][L], v("qk_ready", 1))
                        act.activation(A[L][:, 0:T], R[L][:, 0, 0:T], ACT.Relu).then_inc(S["qT_sb"][L], 1)
                        act.wait_ge(S["v_ready"][L], v("v_ready", 1))
                        act.activation(A[L][:, T:3 * T], R[L][:, 1, :], ACT.Relu).then_inc(S["v_sb"][L], 1)

            def load(dst, src):
                act.dma_start(dst, src, allow_slow_non_contiguous=True).then_inc(c_loaded, 16)

            load(eye[:, :], const("eye"))
            load(stage[:, :], io["consts"][:, 0:N_STAGE])
            load(Tk[:, :, :].rearrange("p c t -> p (c t)"), const("kc"))
            load(lo_q[:, :], const("lo_q"))
            load(lo_k[:, :], const("lo_k"))
            load(block[:, :], const("block"))
            load(parity[:, :], const("parity"))
            load(order[:, :, :].rearrange("p t e -> p (t e)"), const("order"))
            for l in range(DEPTH):
                for g, name in enumerate(("q_scale", "k_scale")):
                    load(scl[:, l, g, 0, :], io[name][l].partition_broadcast(P))
                    for s_ in range(2):
                        a_, b_ = 32 * s_, 32 - 32 * s_
                        load(scl[:, l, g, 1, a_:a_ + 32], io[name][l, b_:b_ + 32].partition_broadcast(P))
            act.wait_ge(ready, 6)
            act.wait_ge(xT_sb, 8)
            ffn(0)
            attn(1)
            ffn(2)
            moe(3)
            lin(4)
            moe(5)

        @block_.vector
        def _(dve):
            steps = [0]

            def link(ins):
                steps[0] += 1
                ins.then_inc(chain, 1)
                dve.wait_ge(chain, steps[0])

            def split(hi, lo, src):
                link(dve.tensor_copy(hi, src))
                return dve.tensor_tensor(lo, src, hi.bitcast(F32), ALU.subtract)

            dve.wait_ge(c_loaded, 16 * N_C)
            link(dve.tensor_copy(eyeb[:, :], eye[:, :]))
            for L in lanes:
                link(dve.memset(mT[L][:, :], 0.0))
            link(dve.tensor_copy(masks[:, :], part("masks")))
            link(dve.tensor_copy(relub[:, :, :].rearrange("p a b -> p (a b)"), part("relu")))
            link(dve.tensor_copy(sel[:, :, :].rearrange("p h j -> p (h j)"), part("sel")))
            link(dve.tensor_copy(slopeb[:, :, :].rearrange("p h j -> p (h j)"), part("slope_eye")))
            rot = part("rot").rearrange("p (t g c d) -> p t g c d", t=TILES, g=2, c=2)
            for l in range(DEPTH):
                for g in range(2):
                    for c in range(2):
                        link(dve.tensor_tensor(
                            tab[:, l, c, :, g, :], rot[:, :, g, c, :],
                            scl[:, l, g, c, :].unsqueeze(1).to_broadcast([P, TILES, DH]), ALU.mult))
            for q in range(8):
                dve.wait_ge(xT_ready, q + 1)
                dve.tensor_copy(X[:, 2 * q:2 * q + 2, :].rearrange("p s t -> p (s t)"), R[q // 4][:, q % 4, :])\
                    .then_inc(xT_sb, 1)
            dve.wait_ge(small_loaded, 16 * N_SMALL)
            link(split(aw_hi[:, :], aw_lo[:, :], raw_small[:, :]))
            link(dve.tensor_scalar(bq[:, :], bq[:, :], float(ADH) ** -0.5, None, ALU.mult))
            for c in range(4):
                link(dve.tensor_scalar(Tq[:, c, :], part("qc"), bq[:, c:c + 1], None, ALU.add))
                link(dve.tensor_scalar(Tk[:, c, :], Tk[:, c, :], bk[:, c:c + 1], None, ALU.add))
            dve.wait_ge(w_loaded, 16 * 7 * DEPTH)
            for l in range(DEPTH):
                link(split(fw_hi[:, l, 0:o1], fw_lo[:, l, 0:o1], raw_qkv[:, l, :]))
                dve.wait_ge(lbw, l + 1)
                link(dve.tensor_tensor(b1[:, l, :], b1[:, l, :], R[0][:, l, 0:2 * HC], ALU.add))
                w1r = raw_rest[l][:, o2 - o1:o3 - o1]
                link(dve.tensor_scalar(w1r, w1r, lng[:, l:l + 1], None, ALU.mult))
                last = split(fw_hi[:, l, o1:FW], fw_lo[:, l, o1:FW], raw_rest[l])
                if l < DEPTH - 1:
                    link(last)
            last.then_inc(fold, 1)
            dve.wait_ge(fold, 1)
            dve.wait_ge(ready, 6)

            def x_in(v, turn):
                for L in lanes:
                    dve.wait_ge(S["x_out"][L], v("x_out", 0))
                    dve.tensor_copy(Xl[L][:, :], X[:, turn * LANES + L, :]).then_inc(S["x_in"][L], 1)

            def center(v, k, L, src):
                dve.wait_ge(S["mean_ready"][L], v("mean_ready", k))
                dve.tensor_tensor(cen[L][:, :], src, R[L][:, 3, 0:T], ALU.subtract).then_inc(S["centered"][L], 1)

            def halves(L):
                return ((slice(0, 64), slice(0, T)), (slice(64, P), slice(1, T + 1)))

            def normed_split(v, k, kh, L):
                dve.wait_ge(S["rstd"][L], v("rstd", k))
                dve.tensor_tensor(cen[L][:, :], cen[L][:, :], rst[L][:, :], ALU.mult).then_inc(S["normed"][L], 1)
                dve.wait_ge(S["normed"][L], v("normed", k))
                dve.tensor_copy(hh[L][:, :], cen[L][:, :]).then_inc(S["h_hi"][L], 1)
                dve.wait_ge(S["h_hi"][L], v("h_hi", kh))
                dve.tensor_tensor(hl[L][:, :], cen[L][:, :], hh[L][:, :].bitcast(F32), ALU.subtract)\
                    .then_inc(S["h_lo"][L], 1)

            def ffn(ph):
                with dve.Fori(0, TURNS) as turn:
                    v = counter(ph, turn)
                    x_in(v, turn)
                    for L in lanes:
                        dve.wait_ge(S["x_in"][L], v("x_in"))
                        center(v, 1, L, Xl[L][:, :])
                    for L in lanes:
                        dve.wait_ge(S["rstd"][L], v("rstd", 1))
                        for r, c in halves(L):
                            last = dve.tensor_tensor(Y[L][r, c], cen[L][r, :], rst[L][r, :], ALU.mult)
                        last.then_inc(S["normed"][L], 1)
                    for l in range(DEPTH):
                        for L in lanes:
                            if l == 0:
                                dve.wait_ge(S["normed"][L], v("normed", 1))
                            else:
                                dve.wait_ge(S["resid2"][L], v("resid2", l))
                            dve.tensor_copy(hh[L][:, :], Y[L][:, 0:T]).then_inc(S["h_hi"][L], 1)
                            dve.wait_ge(S["h_hi"][L], v("h_hi", 2 * l + 1))
                            dve.tensor_tensor(hl[L][:, :], Y[L][:, 0:T], hh[L][:, :].bitcast(F32), ALU.subtract)\
                                .then_inc(S["h_lo"][L], 1)
                        for L in lanes:
                            a = A[L].rearrange("p (g h d) -> p g h d", g=4, h=HEADS)
                            c_ = C[L].rearrange("p (g h d) -> p g h d", g=4, h=HEADS)
                            t = tab[:, l, 0, :, :, :].rearrange("p a b d -> p (a b) d")
                            dve.wait_ge(S["qk_sb"][L], v("qk_sb", l + 1))
                            dve.tensor_tensor(c_, a, t.unsqueeze(2).to_broadcast([P, 4, HEADS, DH]), ALU.mult)\
                                .then_inc(S["t_cos"][L], 1)
                            dve.wait_ge(S["sq_sb"][L], v("sq_sb", l + 1))
                            dve.tensor_reduce(sm[L][:, 0:32], sqs[:, :].rearrange("p (g d) -> p g d", d=DH), AX, ALU.add)\
                                .then_inc(S["ss"][L], 1)
                            dve.wait_ge(S["ss"][L], v("ss", l + 1))
                            dve.tensor_scalar(sm[L][:, 32:64], sm[L][:, 0:32], 1e-24, None, ALU.max)\
                                .then_inc(S["ss_max"][L], 1)
                        for L in lanes:
                            dve.wait_ge(S["t_sin"][L], v("t_sin", l + 1))
                            dve.wait_ge(S["t_cos"][L], v("t_cos", l + 1))
                            dve.tensor_tensor(C[L], C[L], B[L], ALU.add).then_inc(S["t_sum"][L], 1)
                            dve.wait_ge(S["rnorm"][L], v("rnorm", l + 1))
                            dve.wait_ge(S["t_sum"][L], v("t_sum", l + 1))
                            c_ = C[L].rearrange("p (g d) -> p g d", d=DH)
                            dve.tensor_tensor(c_, c_, sm[L][:, 96:128].unsqueeze(2).to_broadcast([P, 32, DH]), ALU.mult)\
                                .then_inc(S["qk_rot"][L], 1)
                        for L in lanes:
                            dve.wait_ge(S["qkT_ready"][L], v("qkT_ready", l + 1))
                            dve.tensor_copy(qkT[L][:, 1].rearrange("p c t -> p (c t)"),
                                            R[L][:, 0:2, :].rearrange("p b n -> p (b n)")).then_inc(S["kT_sb"][L], 1)
                            dve.wait_ge(S["kT_sb"][L], v("kT_sb", l + 1))
                            dve.tensor_copy(qkb[L][:, 1], qkT[L][:, 1]).then_inc(S["k_bf"][L], 1)
                            dve.wait_ge(S["qT_sb"][L], v("qT_sb", l + 1))
                            dve.tensor_copy(qkb[L][:, 0], q_par[L][0])
                            dve.tensor_copy(qkb[L][:, 2], q_par[L][1]).then_inc(S["q_bf"][L], 1)
                        for g in range(3):
                            for L in lanes:
                                dve.wait_ge(S["s_ready"][L], v("s_ready", 3 * l + g + 1))
                                if g == 0:
                                    dst, src = sm[L][:, 128:136], R[L][:, 0:2, :].rearrange("p b (h j) -> p b h j", h=4)
                                    dst = dst.rearrange("p (h b) -> p b h", b=2)
                                else:
                                    b_ = 2 if g == 1 else 0
                                    dst = sm[L][:, 132 + 4 * g:136 + 4 * g].rearrange("p (h b) -> p b h", b=2)
                                    src = R[L][:, b_:b_ + 2, 0:2 * J0W].rearrange("p b (h j) -> p b h j", h=2)
                                dve.tensor_reduce(dst, src, AX, ALU.max, negate=True).then_inc(S["s_max"][L], 1)
                        for L in lanes:
                            dve.wait_ge(S["s_max"][L], v("s_max", 3 * l + 3))
                            mx = sm[L][:, 128:144].rearrange("p (t h) -> p t h", t=TILES)
                            dve.tensor_copy(mneg[L][:, :, 0:HEADS], mx).then_inc(S["m_hi"][L], 1)
                            dve.wait_ge(S["m_hi"][L], v("m_hi", l + 1))
                            dve.tensor_tensor(mneg[L][:, :, HEADS:2 * HEADS], mx, mneg[L][:, :, 0:HEADS],
                                              ALU.subtract).then_inc(S["m_lo"][L], 1)
                        for L in lanes:
                            dve.wait_ge(S["mT_ready"][L], v("mT_ready", l + 1))
                            dve.tensor_copy(mT[L][0:2 * HEADS, :], R[L][0:2 * HEADS, 2, 0:T]).then_inc(S["mT_sb"][L], 1)
                        for L in lanes:
                            dve.wait_ge(S["o_ready"][L], v("o_ready", l + 1))
                            ov = R[L][:, :, :].rearrange("p b (h d) -> p b h d", h=4)
                            rec = sm[L][:, 144:160].rearrange("p (b h) -> p b h", b=4)
                            dve.reciprocal(rec, ov[:, :, :, DH]).then_inc(S["o_rec"][L], 1)
                            dve.wait_ge(S["o_rec"][L], v("o_rec", l + 1))
                            dve.tensor_tensor(O[L].rearrange("p (b h d) -> p b h d", b=4, h=4), ov[:, :, :, 0:DH],
                                              rec.unsqueeze(3).to_broadcast([P, 4, 4, DH]), ALU.mult)\
                                .then_inc(S["o_sb"][L], 1)
                        for L in lanes:
                            dve.wait_ge(S["oT_hi"][L], v("oT_hi", l + 1))
                            dve.tensor_tensor(ol[L][:, :, :].rearrange("p c t -> p (c t)"),
                                              R[L][:, 0:2, :].rearrange("p b n -> p (b n)"),
                                              oh[L][:, :, :].rearrange("p c t -> p (c t)").bitcast(F32),
                                              ALU.subtract).then_inc(S["oT_lo"][L], 1)
                        for L in lanes:
                            dve.wait_ge(S["proj_ready"][L], v("proj_ready", l + 1))
                            for r, c in halves(L):
                                last = dve.tensor_tensor(Y[L][r, c], Y[L][r, c], R[L][r, 2, 0:T], ALU.add)
                            last.then_inc(S["resid"][L], 1)
                        for L in lanes:
                            dve.wait_ge(S["resid"][L], v("resid", l + 1))
                            center(v, 2 + l, L, Y[L][:, 0:T])
                        for L in lanes:
                            normed_split(v, 2 + l, 2 * l + 2, L)
                        for L in lanes:
                            dve.wait_ge(S["gelu_sb"][L], v("gelu_sb", l + 1))
                            for c in range(HC):
                                last = dve.scalar_tensor_tensor(
                                    out=U[L][:, c, :], in0=R[L][:, c // 2, (c % 2) * T:(c % 2 + 1) * T],
                                    scalar=b1[:, l, c:c + 1], in1=G[L][:, c, :], op0=ALU.add, op1=ALU.mult)
                            last.then_inc(S["u_sb"][L], 1)
                            dve.wait_ge(S["u_sb"][L], v("u_sb", l + 1))
                            dve.tensor_copy(oh[L][:, 0:HC, :], U[L][:, :, :]).then_inc(S["u_hi"][L], 1)
                            dve.wait_ge(S["u_hi"][L], v("u_hi", l + 1))
                            dve.tensor_tensor(ol[L][:, 0:HC, :], U[L][:, :, :], oh[L][:, 0:HC, :].bitcast(F32),
                                              ALU.subtract).then_inc(S["u_lo"][L], 1)
                        for L in lanes:
                            dve.wait_ge(S["down_ready"][L], v("down_ready", l + 1))
                            for r, c in halves(L):
                                last = dve.scalar_tensor_tensor(
                                    out=Y[L][r, c], in0=R[L][r, 0, 0:T], scalar=b2[r, l:l + 1], in1=Y[L][r, c],
                                    op0=ALU.add, op1=ALU.add)
                            last.then_inc(S["resid2"][L], 1)
                    for L in lanes:
                        dve.wait_ge(S["resid2"][L], v("resid2", DEPTH))
                        for r, c in halves(L):
                            last = dve.scalar_tensor_tensor(
                                out=X[r, turn * LANES + L, :], in0=Y[L][r, c], scalar=0.5, in1=Xl[L][r, :],
                                op0=ALU.mult, op1=ALU.add)
                        last.then_inc(S["x_out"][L], 1)

            def ln_front(ph, v, turn):
                x_in(v, turn)
                for L in lanes:
                    dve.wait_ge(S["x_in"][L], v("x_in"))
                    center(v, 1, L, Xl[L][:, :])
                for L in lanes:
                    normed_split(v, 1, 1, L)

            def attn(ph):
                with dve.Fori(0, TURNS) as turn:
                    v = counter(ph, turn)
                    ln_front(ph, v, turn)
                    for L in lanes:
                        dve.wait_ge(S["qk_ready"][L], v("qk_ready"))
                        for g, (buf, tb, s) in enumerate(((A, Tq, float(ADH) ** -0.5), (B, Tk, 1.0))):
                            dve.scalar_tensor_tensor(
                                out=buf[L][:, 0:1024], in0=R[L][:, 2 * g:2 * g + 2, :].rearrange("p b n -> p (b n)"),
                                scalar=s, in1=tb[:, :, :].rearrange("p c t -> p (c t)"), op0=ALU.mult, op1=ALU.add)\
                                .then_inc(S["t_cos"][L], 1)
                    for L in lanes:
                        for g, (buf, hi, lo) in enumerate(((A, ol, lo_q), (B, oh, lo_k))):
                            dve.wait_ge(S["qT_sb"][L], v("qT_sb", g + 1))
                            hi_ = hi[L][:, :, :].rearrange("p c t -> p (c t)")
                            dve.scalar_tensor_tensor(
                                out=hi_, in0=hi_.bitcast(F32), scalar=lo[:, 0:1],
                                in1=buf[L][:, 0:1024], op0=ALU.mult, op1=ALU.add).then_inc(S["qk_rot"][L], 1)
                        dve.wait_ge(S["v_ready"][L], v("v_ready"))
                        dve.tensor_tensor(AV(L)[:, :, :, 0:ADH],
                                          R[L][:, 0, 0:T].rearrange("p (t h d) -> p t h d", t=TILES, h=AH),
                                          bv[:, :].rearrange("p (h d) -> p h d", h=AH).unsqueeze(1)
                                          .to_broadcast([P, TILES, AH, ADH]), ALU.add).then_inc(S["v_sb"][L], 1)
                    for q in range(4):
                        for L in lanes:
                            dve.wait_ge(S["s_ready"][L], v("s_ready", q + 1))
                            dst = sm[L][:, 0:TILES * AH].rearrange("p (t h) -> p h t", t=TILES)[:, 4 * q:4 * q + 4, :]
                            dve.tensor_reduce(dst, R[L][:, :, :].rearrange("p b (t j) -> p b t j", t=TILES), AX,
                                              ALU.max, negate=True).then_inc(S["s_max"][L], 1)
                    for L in lanes:
                        dve.wait_ge(S["s_max"][L], v("s_max", 4))
                        mx = sm[L][:, 0:TILES * AH].rearrange("p (t h) -> p t h", t=TILES)
                        dve.tensor_copy(mpad[L][:, :, :, ROW_MHI], mx).then_inc(S["m_hi"][L], 1)
                        dve.wait_ge(S["m_hi"][L], v("m_hi"))
                        dve.tensor_tensor(mpad[L][:, :, :, ROW_MLO], mx, mpad[L][:, :, :, ROW_MHI],
                                          ALU.subtract).then_inc(S["m_lo"][L], 1)
                    for L in lanes:
                        dve.wait_ge(S["mT_ready"][L], v("mT_ready"))
                        q_ = ol[L][:, :, :].rearrange("p c t -> p (c t)")
                        dve.tensor_tensor(q_, q_.bitcast(F32), R[L][:, 0:2, :].rearrange("p b n -> p (b n)"), ALU.add)\
                            .then_inc(S["mT_sb"][L], 1)
                    for L in lanes:
                        dve.wait_ge(S["o_ready"][L], v("o_ready", AH))
                        ov = lambda t: R[L][:, 3, t * O_TILE:t * O_TILE + AH * (ADH + 1)]\
                            .rearrange("p (h d) -> p h d", d=ADH + 1)
                        rec = lambda t: sm[L][:, 64 + t * AH:64 + (t + 1) * AH]
                        for t in range(TILES):
                            last = dve.reciprocal(rec(t), ov(t)[:, :, ADH])
                        last.then_inc(S["o_rec"][L], 1)
                        dve.wait_ge(S["o_rec"][L], v("o_rec"))
                        for t in range(TILES):
                            last = dve.tensor_tensor(A[L][:, t * P:(t + 1) * P].rearrange("p (h d) -> p h d", d=ADH),
                                                     ov(t)[:, :, 0:ADH],
                                                     rec(t).unsqueeze(2).to_broadcast([P, AH, ADH]), ALU.mult)
                        last.then_inc(S["o_sb"][L], 1)
                    for L in lanes:
                        dve.wait_ge(S["oT_hi"][L], v("oT_hi"))
                        dve.tensor_tensor(hl[L][:, :], R[L][:, 0, 0:T], hh[L][:, :].bitcast(F32), ALU.subtract)\
                            .then_inc(S["oT_lo"][L], 1)
                    for L in lanes:
                        dve.wait_ge(S["proj_ready"][L], v("proj_ready"))
                        dve.scalar_tensor_tensor(out=X[:, turn * LANES + L, :], in0=R[L][:, 1, 0:T], scalar=ab[:, 0:1],
                                                 in1=Xl[L][:, :], op0=ALU.add, op1=ALU.add).then_inc(S["x_out"][L], 1)

            def moe(ph):
                with dve.Fori(0, TURNS) as turn:
                    v = counter(ph, turn)
                    ln_front(ph, v, turn)
                    for L in lanes:
                        s3 = lambda a: sm[L][:, a:a + TILES * NE].rearrange("p (t e) -> p t e", t=TILES)
                        bc = lambda a: sm[L][:, a:a + TILES].unsqueeze(2).to_broadcast([P, TILES, NE])
                        dve.wait_ge(S["qk_ready"][L], v("qk_ready"))
                        dve.tensor_tensor(s3(0), R[L][:, 3, 0:TILES * NE].rearrange("p (t e) -> p t e", t=TILES),
                                          br[:, :, :], ALU.add).then_inc(S["ss"][L], 1)
                        dve.wait_ge(S["ss"][L], v("ss"))
                        dve.tensor_reduce(sm[L][:, 16:18], s3(0), AX, ALU.max).then_inc(S["ss_max"][L], 1)
                        dve.wait_ge(S["ss_max"][L], v("ss_max"))
                        dve.tensor_tensor(s3(32), s3(0), bc(16), ALU.is_ge).then_inc(S["t_cos"][L], 1)
                        dve.wait_ge(S["t_cos"][L], v("t_cos"))
                        dve.tensor_tensor(s3(48), s3(32), order[:, :, :], ALU.mult).then_inc(S["t_sin"][L], 1)
                        dve.wait_ge(S["t_sin"][L], v("t_sin"))
                        dve.tensor_reduce(sm[L][:, 18:20], s3(48), AX, ALU.max).then_inc(S["t_sum"][L], 1)
                        dve.wait_ge(S["t_sum"][L], v("t_sum"))
                        dve.tensor_tensor(s3(64), s3(48), bc(18), ALU.is_ge).then_inc(S["qk_rot"][L], 1)
                    for L in lanes:
                        dve.wait_ge(S["qkT_ready"][L], v("qkT_ready"))
                        dve.tensor_copy(B[L][0:NE, 0:T], R[L][0:NE, 3, T:2 * T]).then_inc(S["mT_sb"][L], 1)
                    for L in lanes:
                        dve.wait_ge(S["mT_ready"][L], v("mT_ready"))
                        dve.tensor_copy(B[L][:, T:2 * T], R[L][:, 3, 0:T]).then_inc(S["u_sb"][L], 1)
                    for e in range(NE):
                        for L in lanes:
                            dve.wait_ge(S["gelu_sb"][L], v("gelu_sb", e + 1))
                            if e:
                                dve.wait_ge(S["down_ready"][L], v("down_ready", e))
                            dve.tensor_copy(oh[L][:, :, :], EG(L)).then_inc(S["u_hi"][L], 1)
                            dve.wait_ge(S["u_hi"][L], v("u_hi", e + 1))
                            dve.tensor_tensor(ol[L][:, :, :], EG(L), oh[L][:, :, :].bitcast(F32), ALU.subtract)\
                                .then_inc(S["u_lo"][L], 1)
                        for L in lanes:
                            dve.wait_ge(S["down_ready"][L], v("down_ready", e + 1))
                            dve.wait_ge(S["u_sb"][L], v("u_sb", e + 1))
                            for t in range(TILES):
                                acc = B[L][:, T + t * P:T + (t + 1) * P]
                                last = dve.scalar_tensor_tensor(
                                    out=acc, in0=R[L][:, 2, t * P:(t + 1) * P],
                                    scalar=sm[L][:, 64 + t * NE + e:65 + t * NE + e], in1=acc,
                                    op0=ALU.mult, op1=ALU.add)
                            last.then_inc(S["u_sb"][L], 1)
                    for L in lanes:
                        dve.wait_ge(S["oT_ready"][L], v("oT_ready"))
                        dve.scalar_tensor_tensor(out=X[:, turn * LANES + L, :], in0=R[L][:, 3, 0:T], scalar=0.5,
                                                 in1=Xl[L][:, :], op0=ALU.mult, op1=ALU.add)\
                            .then_inc(S["x_out"][L], 1)

            def lin(ph):
                with dve.Fori(0, TURNS) as turn:
                    v = counter(ph, turn)
                    ln_front(ph, v, turn)
                    for L in lanes:
                        dve.wait_ge(S["s_ready"][L], v("s_ready"))
                        dve.tensor_tensor(B[L][:, 0:P], R[L][:, 2, 0:P], block[:, :], ALU.mult).then_inc(S["m_hi"][L], 1)
                        dve.tensor_scalar(B[L][:, P:2 * P], block[:, :], R[L][:, 2, P:P + 1], None, ALU.mult)\
                            .then_inc(S["m_lo"][L], 1)
                    for L in lanes:
                        dve.wait_ge(S["o_ready"][L], v("o_ready"))
                        dve.tensor_scalar(B[L][:, T:2 * T], R[L][:, 3, T:2 * T], 1e-15, None, ALU.add)\
                            .then_inc(S["t_sum"][L], 1)
                        dve.wait_ge(S["t_sum"][L], v("t_sum"))
                        dve.reciprocal(B[L][:, 2 * T:3 * T], B[L][:, T:2 * T]).then_inc(S["o_rec"][L], 1)
                        dve.wait_ge(S["o_rec"][L], v("o_rec"))
                        dve.tensor_tensor(B[L][:, 3 * T:4 * T], R[L][:, 3, 0:T], B[L][:, 2 * T:3 * T], ALU.mult)\
                            .then_inc(S["o_sb"][L], 1)
                        dve.wait_ge(S["o_sb"][L], v("o_sb"))
                        dve.tensor_copy(oh[L][:, 0, :], B[L][:, 3 * T:4 * T]).then_inc(S["oT_hi"][L], 1)
                        dve.wait_ge(S["oT_hi"][L], v("oT_hi"))
                        dve.tensor_tensor(ol[L][:, 0, :], B[L][:, 3 * T:4 * T], oh[L][:, 0, :].bitcast(F32),
                                          ALU.subtract).then_inc(S["oT_lo"][L], 1)
                    for L in lanes:
                        dve.wait_ge(S["proj_ready"][L], v("proj_ready"))
                        dve.scalar_tensor_tensor(out=X[:, turn * LANES + L, :], in0=R[L][:, 0, 0:T], scalar=lb_[:, 0:1],
                                                 in1=Xl[L][:, :], op0=ALU.add, op1=ALU.add).then_inc(S["x_out"][L], 1)

            ffn(0)
            for L in lanes:
                link(dve.memset(AV(L), 1.0))
                link(dve.memset(mpad[L], 0.0))
            attn(1)
            for L in lanes:
                link(dve.memset(Vw[L][:, :], 1.0))
            ffn(2)
            dve.wait_ge(ew_loaded, 48)
            for w in range(2):
                link(split(ew_hi[:, w], ew_lo[:, w], raw_e[w]))
            split(lw_hi[:, :], lw_lo[:, :], raw_lin).then_inc(ew_split, 1)
            moe(3)
            lin(4)
            moe(5)
            for q in range(8):
                dve.wait_ge(xo_ready, q + 1)
                dve.tensor_copy(xin[:, 4 * q:4 * q + 4, :].rearrange("p n d -> p (n d)"), R[q // 4][:, q % 4, :])\
                    .then_inc(xo_sb, 1)

        @block_.tensor
        def _(pe):
            def three(out, w_hi, w_lo, x_hi, x_lo, first, last):
                pe.matmul(out, w_hi, x_hi, start=first, stop=False)
                pe.matmul(out, w_lo, x_hi, start=False, stop=False)
                return pe.matmul(out, w_hi, x_lo, start=False, stop=last)

            def mean(v, k, L, src):
                pe.matmul(R[L][:, 3, 0:T], ones[:, :], src, start=True, stop=True).then_inc(S["mean_ready"][L], 1)

            def var(v, k, L):
                pe.wait_ge(S["squared"][L], v("squared", k))
                pe.matmul(R[L][:, 3, T:2 * T], ones[:, :], sqr[L][:, :], start=True, stop=True)\
                    .then_inc(S["var_ready"][L], 1)

            def outer_norm(v):
                for L in lanes:
                    pe.wait_ge(S["x_in"][L], v("x_in"))
                    mean(v, 1, L, Xl[L][:, :])
                for L in lanes:
                    var(v, 1, L)

            pe.wait_ge(c_loaded, 16 * N_C)
            for q in range(8):
                if q % 2 == 0:
                    pe.wait_ge(x_loaded, 16 * 4)
                for n in range(4):
                    last = pe.transpose(R[q // 4][:, q % 4, n * P:(n + 1) * P], xin[:, 4 * q + n, :], eye[:, :])
                last.then_inc(xT_ready, 1)
            pe.wait_ge(w_loaded, 16 * 7 * DEPTH)
            pe.wait_ge(small_loaded, 16 * N_SMALL)
            pe.wait_ge(xT_sb, 8)
            for l in range(DEPTH):
                for c in range(2 * HC):
                    a = o2 - o1 + c * P
                    last = pe.matmul(R[0][:, l, c:c + 1], raw_rest[l][:, a:a + P], lnb[:, l:l + 1], start=True, stop=True)
                last.then_inc(lbw, 1)
            pe.wait_ge(fold, 1)

            def ffn(ph):
                with pe.Fori(0, TURNS) as turn:
                    v = counter(ph, turn)
                    outer_norm(v)
                    for l in range(DEPTH):
                        wh, wl = fw_hi[:, l, :], fw_lo[:, l, :]
                        for L in lanes:
                            pe.wait_ge(S["h_lo"][L], v("h_lo", 2 * l + 1))
                            for t in range(TILES):
                                ts_ = slice(t * P, (t + 1) * P)
                                for g in range(2):
                                    ws = slice(g * INNER, (g + 1) * INNER)
                                    last = three(R[L][:, 2 * t + g, :], hh[L][:, ts_], hl[L][:, ts_], wh[:, ws], wl[:, ws],
                                                 True, True)
                            last.then_inc(S["qk_ready"][L], 1)
                        for L in lanes:
                            pe.wait_ge(S["qk_sb"][L], v("qk_sb", l + 1))
                            for t in range(TILES):
                                ts_, ws = slice(t * P, (t + 1) * P), slice(2 * INNER, 3 * INNER)
                                last = three(R[L][:, t, :], hh[L][:, ts_], hl[L][:, ts_], wh[:, ws], wl[:, ws], True, True)
                            last.then_inc(S["v_ready"][L], 1)
                        for L in lanes:
                            pe.wait_ge(S["qk_rot"][L], v("qk_rot", l + 1))
                            pe.wait_ge(S["v_sb"][L], v("v_sb", l + 1))
                            for g in range(2):
                                for c in range(4):
                                    for t in range(TILES):
                                        src = C[L].rearrange("p (t g n) -> p t g n", t=TILES, g=2)[:, t, g, c * P:(c + 1) * P]
                                        o = (c % 2) * T + t * P
                                        last = pe.transpose(R[L][:, 2 - 2 * g + c // 2, o:o + P], src, eye[:, :])
                            last.then_inc(S["qkT_ready"][L], 1)
                        for g in range(3):
                            for L in lanes:
                                if g == 0:
                                    pe.wait_ge(S["k_bf"][L], v("k_bf", l + 1))
                                    pe.wait_ge(S["q_bf"][L], v("q_bf", l + 1))
                                    w, per, hs, bank, m, tq, k0 = P, 4, range(8), 0, ms0, 0, 0
                                else:
                                    if g == 2:
                                        pe.wait_ge(S["s_max"][L], v("s_max", 3 * l + 1))
                                    w, per, tq, k0, m = J0W, 2, 1, WIN, ms1
                                    bank, hs = (2, range(4)) if g == 1 else (0, range(4, 8))
                                for i, h in enumerate(hs):
                                    b_, o = bank + i % 2, (i // 2) * w
                                    if i < 2:
                                        pe.matmul(R[L][:, b_, 0:per * w], eyeb[:, :],
                                                  m.unsqueeze(1).to_broadcast([P, per, w]),
                                                  start=True, stop=False, skip_group_check=True)
                                    last = pe.matmul(R[L][:, b_, o:o + w],
                                                     qkb[L][:, 2 * (h % 2), h // 2, tq * P:(tq + 1) * P],
                                                     qkb[L][:, 1, h // 2, k0:k0 + w], start=False,
                                                     stop=True, skip_group_check=True)
                                last.then_inc(S["s_ready"][L], 1)
                        for L in lanes:
                            pe.wait_ge(S["m_lo"][L], v("m_lo", l + 1))
                            for t in range(TILES):
                                last = pe.matmul(R[L][0:2 * HEADS, 2, t * P:(t + 1) * P], mneg[L][:, t, :], eyeb[:, :],
                                                 start=True, stop=True)
                            last.then_inc(S["mT_ready"][L], 1)
                        for L in lanes:
                            pe.wait_ge(S["mT_sb"][L], v("mT_sb", l + 1))
                            for k in range(6):
                                if k >= 4:
                                    pe.wait_ge(S["p_sb"][L], v("p_sb", 6 * l + k - 3))
                                hs = ST_HEADS[k]
                                jt = len(hs) // 4
                                w, i0, m = (J1W, P, mst1) if jt else (J0W, 0, mst0)
                                for i, h in enumerate(hs):
                                    pe.matmul(R[L][:, k % 4, i * w:(i + 1) * w], sel[:, h, :], mT[L][:, i0:i0 + w],
                                              start=i == 0, stop=False, skip_group_check=True)
                                pe.matmul(R[L][:, k % 4, 0:len(hs) * w], eyeb[:, :],
                                          m.unsqueeze(1).to_broadcast([P, len(hs), w]), start=False, stop=False,
                                          skip_group_check=True)
                                for i, h in enumerate(hs):
                                    last = pe.matmul(R[L][:, k % 4, i * w:(i + 1) * w],
                                                     qkT[L][:, 1, h // 2, jt * P:(jt + 1) * P],
                                                     q_par[L][h % 2][:, h // 2, i0:i0 + w], start=False, stop=True,
                                                     skip_group_check=True)
                                last.then_inc(S["st_ready"][L], 1)
                        for L in lanes:
                            pe.wait_ge(S["p_sb"][L], v("p_sb", 6 * l + 6))
                            for h in range(HEADS):
                                o = (h % 4) * P
                                out = lambda t: R[L][:, 2 * t + h // 4, o:o + P]
                                win = lambda t: Vw[L][:, (t * HEADS + h) * (DH + 1):(t * HEADS + h) * (DH + 1) + P]
                                pe.matmul(out(0), PT[L][:, h, 0:P], win(0), start=True, stop=True)
                                pe.matmul(out(1), PT[L][:, h, J0W:JW], win(1), start=True, stop=False,
                                          skip_group_check=True)
                                last = pe.matmul(out(1)[0:WIN, :], PT[L][:, h, P:J0W], win(0), start=False,
                                                 stop=True, skip_group_check=True)
                            last.then_inc(S["o_ready"][L], 1)
                        for L in lanes:
                            pe.wait_ge(S["o_sb"][L], v("o_sb", l + 1))
                            for c in range(4):
                                for t in range(TILES):
                                    a = t * INNER + c * P
                                    o = (c % 2) * T + t * P
                                    last = pe.transpose(R[L][:, c // 2, o:o + P], O[L][:, a:a + P], eye[:, :])
                            last.then_inc(S["oT_ready"][L], 1)
                        for L in lanes:
                            pe.wait_ge(S["oT_lo"][L], v("oT_lo", l + 1))
                            for c in range(4):
                                ws = slice(o1 + c * P, o1 + (c + 1) * P)
                                last = three(R[L][:, 2, 0:T], wh[:, ws], wl[:, ws], oh[L][:, c, :], ol[L][:, c, :],
                                             c == 0, c == 3)
                            last.then_inc(S["proj_ready"][L], 1)
                        for L in lanes:
                            pe.wait_ge(S["resid"][L], v("resid", l + 1))
                            mean(v, 2 + l, L, Y[L][:, 0:T])
                        for L in lanes:
                            var(v, 2 + l, L)
                        for L in lanes:
                            pe.wait_ge(S["h_lo"][L], v("h_lo", 2 * l + 2))
                            for c in range(2 * HC):
                                ws = slice(o2 + c * P, o2 + (c + 1) * P)
                                g, cc = c // HC, c % HC
                                last = three(R[L][:, 2 * g + cc // 2, (cc % 2) * T:(cc % 2 + 1) * T], wh[:, ws], wl[:, ws],
                                             hh[L][:, :], hl[L][:, :], True, True)
                            last.then_inc(S["up_ready"][L], 1)
                        for L in lanes:
                            pe.wait_ge(S["u_lo"][L], v("u_lo", l + 1))
                            for c in range(HC):
                                ws = slice(o3 + c * P, o3 + (c + 1) * P)
                                last = three(R[L][:, 0, 0:T], wh[:, ws], wl[:, ws], oh[L][:, c, :], ol[L][:, c, :],
                                             c == 0, c == HC - 1)
                            last.then_inc(S["down_ready"][L], 1)

            def attn(ph):
                wq, wk, wv, wo = 0, 4 * P, 8 * P, 9 * P
                with pe.Fori(0, TURNS) as turn:
                    v = counter(ph, turn)
                    outer_norm(v)
                    for L in lanes:
                        pe.wait_ge(S["h_lo"][L], v("h_lo"))
                        for g, w in enumerate((wq, wk)):
                            for c in range(4):
                                ws = slice(w + c * P, w + (c + 1) * P)
                                last = three(R[L][:, 2 * g + c // 2, (c % 2) * T:(c % 2 + 1) * T], aw_hi[:, ws],
                                             aw_lo[:, ws], hh[L][:, :], hl[L][:, :], True, True)
                        last.then_inc(S["qk_ready"][L], 1)
                    for L in lanes:
                        pe.wait_ge(S["t_cos"][L], v("t_cos", 2))
                        for t in range(TILES):
                            ts_, ws = slice(t * P, (t + 1) * P), slice(wv, wv + P)
                            last = three(R[L][:, 0, ts_], hh[L][:, ts_], hl[L][:, ts_], aw_hi[:, ws], aw_lo[:, ws],
                                         True, True)
                        last.then_inc(S["v_ready"][L], 1)
                    for q in range(4):
                        for L in lanes:
                            if q == 0:
                                pe.wait_ge(S["v_sb"][L], v("v_sb"))
                            else:
                                pe.wait_ge(S["s_max"][L], v("s_max", q))
                            for s in range(4):
                                r = slice(SLOT * s, SLOT * s + SLOT)
                                for t in range(TILES):
                                    pe.matmul(R[L][:, s, t * T:(t + 1) * T], ol[L][r, q, t * P:(t + 1) * P], oh[L][r, q, :],
                                              start=t == 0, stop=False, skip_group_check=True)
                            for s in range(4):
                                for t in range(TILES):
                                    a = t * T + t * P
                                    last = pe.matmul(R[L][:, s, a:a + P], slopeb[:, 4 * q + s, :],
                                                     relub[:, 1 - t, :], start=False, stop=True, skip_group_check=True)
                            last.then_inc(S["s_ready"][L], 1)
                    for L in lanes:
                        pe.wait_ge(S["m_lo"][L], v("m_lo"))
                        for c in range(4):
                            for t in range(TILES):
                                o = (c % 2) * T + t * P
                                last = pe.matmul(R[L][:, c // 2, o:o + P],
                                                 mpad[L][:, t, 4 * c:4 * c + 4, :].rearrange("p h r -> p (h r)"),
                                                 eyeb[:, :], start=True, stop=True)
                        last.then_inc(S["mT_ready"][L], 1)
                    for t in range(AH + 2):
                        if t < AH:
                            for L in lanes:
                                if t == 0:
                                    pe.wait_ge(S["mT_sb"][L], v("mT_sb"))
                                if t >= 3:
                                    pe.wait_ge(S["p_sb"][L], v("p_sb", t - 2))
                                r = slice(SLOT * (t % 4), SLOT * (t % 4) + SLOT)
                                for j in range(TILES):
                                    pe.matmul(R[L][:, t % 3, j * T:(j + 1) * T], oh[L][r, t // 4, j * P:(j + 1) * P],
                                              ol[L][r, t // 4, :], start=j == 0, stop=False, skip_group_check=True)
                                for j in range(TILES):
                                    a = j * T + j * P
                                    last = pe.matmul(R[L][:, t % 3, a:a + P], slopeb[:, t, :], relub[:, j, :],
                                                     start=False, stop=True, skip_group_check=True)
                                last.then_inc(S["st_ready"][L], 1)
                        if t >= 2:
                            h = t - 2
                            for L in lanes:
                                pe.wait_ge(S["p_sb"][L], v("p_sb", h + 1))
                                for i in range(TILES):
                                    o = i * O_TILE + h * (ADH + 1)
                                    n = min(P, 512 - o)
                                    for j in range(TILES):
                                        a = (j * AH + h) * (ADH + 1)
                                        last = pe.matmul(R[L][:, 3, o:o + n],
                                                         APT(L, h)[:, j * T + i * P:j * T + (i + 1) * P],
                                                         Vw[L][:, a:a + n], start=j == 0, stop=j == 1)
                                last.then_inc(S["o_ready"][L], 1)
                    for L in lanes:
                        pe.wait_ge(S["o_sb"][L], v("o_sb"))
                        for t in range(TILES):
                            last = pe.transpose(R[L][:, 0, t * P:(t + 1) * P], A[L][:, t * P:(t + 1) * P], eye[:, :])
                        last.then_inc(S["oT_ready"][L], 1)
                    for L in lanes:
                        pe.wait_ge(S["oT_lo"][L], v("oT_lo"))
                        ws = slice(wo, wo + P)
                        three(R[L][:, 1, 0:T], aw_hi[:, ws], aw_lo[:, ws], hh[L][:, :], hl[L][:, :], True, True)\
                            .then_inc(S["proj_ready"][L], 1)

            def moe(ph):
                with pe.Fori(0, TURNS) as turn:
                    v = counter(ph, turn)
                    outer_norm(v)
                    for L in lanes:
                        pe.wait_ge(S["h_lo"][L], v("h_lo"))
                        for t in range(TILES):
                            last = pe.matmul(R[L][:, 3, t * NE:(t + 1) * NE], cen[L][:, t * P:(t + 1) * P], wr[:, :],
                                             start=True, stop=True)
                        last.then_inc(S["qk_ready"][L], 1)
                    for L in lanes:
                        pe.wait_ge(S["qk_rot"][L], v("qk_rot"))
                        for t in range(TILES):
                            a = 64 + t * NE
                            last = pe.transpose(R[L][0:NE, 3, T + t * P:T + (t + 1) * P], sm[L][:, a:a + NE], eye[:, :])
                        last.then_inc(S["qkT_ready"][L], 1)
                    for L in lanes:
                        pe.wait_ge(S["mT_sb"][L], v("mT_sb"))
                        for t in range(TILES):
                            last = pe.matmul(R[L][:, 3, t * P:(t + 1) * P], B[L][0:NE, t * P:(t + 1) * P], eb2[:, :],
                                             start=True, stop=True)
                        last.then_inc(S["mT_ready"][L], 1)
                    for e in range(NE + 1):
                        for L in lanes:
                            if e < NE:
                                if e:
                                    pe.wait_ge(S["gelu_sb"][L], v("gelu_sb", e))
                                for c in range(EC):
                                    ws = slice(c * P, (c + 1) * P)
                                    last = three(R[L][:, c // 2, (c % 2) * T:(c % 2 + 1) * T], ew_hi[:, 0, e, ws],
                                                 ew_lo[:, 0, e, ws], hh[L][:, :], hl[L][:, :], True, True)
                                last.then_inc(S["up_ready"][L], 1)
                        for L in lanes:
                            if e:
                                pe.wait_ge(S["u_lo"][L], v("u_lo", e))
                                pe.wait_ge(S["u_sb"][L], v("u_sb", e))
                                for t in range(TILES):
                                    for c in range(EC):
                                        ws, ts_ = slice(c * P, (c + 1) * P), slice(t * P, (t + 1) * P)
                                        last = three(R[L][:, 2, ts_], oh[L][:, c, ts_], ol[L][:, c, ts_],
                                                     ew_hi[:, 1, e - 1, ws], ew_lo[:, 1, e - 1, ws], c == 0, c == EC - 1)
                                last.then_inc(S["down_ready"][L], 1)
                    for L in lanes:
                        pe.wait_ge(S["u_sb"][L], v("u_sb", NE + 1))
                        for t in range(TILES):
                            last = pe.transpose(R[L][:, 3, t * P:(t + 1) * P], B[L][:, T + t * P:T + (t + 1) * P], eye[:, :])
                        last.then_inc(S["oT_ready"][L], 1)

            def lin(ph):
                wq, wkv, wp = 0, P, 3 * P
                with pe.Fori(0, TURNS) as turn:
                    v = counter(ph, turn)
                    outer_norm(v)
                    for L in lanes:
                        pe.wait_ge(S["h_lo"][L], v("h_lo"))
                        three(R[L][:, 0, 0:T], lw_hi[:, wq:wq + P], lw_lo[:, wq:wq + P], hh[L][:, :], hl[L][:, :],
                              True, True).then_inc(S["qk_ready"][L], 1)
                        for t in range(TILES):
                            ts_, ws = slice(t * P, (t + 1) * P), slice(wkv, wkv + 2 * P)
                            last = three(R[L][:, 1, t * T:(t + 1) * T], hh[L][:, ts_], hl[L][:, ts_], lw_hi[:, ws],
                                         lw_lo[:, ws], True, True)
                        last.then_inc(S["v_ready"][L], 1)
                    for L in lanes:
                        pe.wait_ge(S["v_sb"][L], v("v_sb"))
                        k = lambda t: A[L][:, T + t * T:T + t * T + P]
                        for t in range(TILES):
                            pe.matmul(R[L][:, 2, 0:P], k(t), A[L][:, T + t * T + P:T + t * T + 2 * P],
                                      start=t == 0, stop=t == 1)
                        for t in range(TILES):
                            last = pe.matmul(R[L][:, 2, P:P + 1], k(t), one_col[:, 0:1], start=t == 0, stop=t == 1)
                        last.then_inc(S["s_ready"][L], 1)
                    for L in lanes:
                        pe.wait_ge(S["m_lo"][L], v("m_lo"))
                        pe.matmul(R[L][:, 3, 0:T], B[L][:, 0:P], A[L][:, 0:T], start=True, stop=True)
                        pe.matmul(R[L][:, 3, T:2 * T], B[L][:, P:2 * P], A[L][:, 0:T], start=True, stop=True)\
                            .then_inc(S["o_ready"][L], 1)
                    for L in lanes:
                        pe.wait_ge(S["oT_lo"][L], v("oT_lo"))
                        three(R[L][:, 0, 0:T], lw_hi[:, wp:wp + P], lw_lo[:, wp:wp + P], oh[L][:, 0, :], ol[L][:, 0, :],
                              True, True).then_inc(S["proj_ready"][L], 1)

            ffn(0)
            attn(1)
            ffn(2)
            pe.wait_ge(ew_split, 1)
            moe(3)
            lin(4)
            moe(5)
            for L in lanes:
                pe.wait_ge(S["x_out"][L], counter(len(PHASES) - 1, TURNS)("x_out", 0))
            for q in range(8):
                for n in range(4):
                    m = 4 * q + n
                    last = pe.transpose(R[q // 4][:, q % 4, n * P:(n + 1) * P], X[:, m // 2, (m % 2) * P:(m % 2 + 1) * P],
                                        eye[:, :])
                last.then_inc(xo_ready, 1)


def kernel(**inputs):
    import concourse.bacc as bacc
    from concourse.bass_utils import run_bass_kernel_spmd

    f = {k: np.ascontiguousarray(a) for k, a in inputs.items()}
    consts, at = shape_constants()

    w = f["L0_attn_qkv_w"].reshape(AH, 3, ADH, D)
    bias = f["L0_attn_qkv_b"].reshape(AH, 3, ADH)
    slots_w = np.zeros((2, AH, SLOT, D), w.dtype)
    slots_b = np.zeros((2, AH, SLOT), w.dtype)
    for g in range(2):
        for r in range(3):
            slots_w[g, :, r * ADH:(r + 1) * ADH] = w[:, g]
            slots_b[g, :, r * ADH:(r + 1) * ADH] = bias[:, g]
    attn_w = np.concatenate([slots_w.reshape(-1, D), w[:, 2].reshape(-1, D), f["L0_attn_out_w"]], 0).T
    lin_w = np.concatenate([f["L1_attn_qkv_weight"], f["L1_attn_proj_weight"]], 0).T
    arrays = dict(
        x=f["L0_attn_x"], consts=consts, attn_w=attn_w, lin_w=lin_w,
        bias_q=slots_b[0].reshape(4, P).T, bias_k=slots_b[1].reshape(4, P).T, bias_v=bias[:, 2].reshape(-1),
        attn_out_b=f["L0_attn_out_b"], proj_b=f["L1_attn_proj_bias"],
        wqkv=f["L0_ffn_wqkv"], q_scale=f["L0_ffn_q_scale"], k_scale=f["L0_ffn_k_scale"], wo=f["L0_ffn_wo"],
        ln_g=f["L0_ffn_ln_g"], ln_b=f["L0_ffn_ln_b"], w1=f["L0_ffn_w1"], b1=f["L0_ffn_b1"], w2=f["L0_ffn_w2"],
        b2=f["L0_ffn_b2"], wr=f["L1_ffn_wr"], br=f["L1_ffn_br"], ew1=f["L1_ffn_w1"], eb1=f["L1_ffn_b1"],
        ew2=f["L1_ffn_w2"], eb2=f["L1_ffn_b2"])
    arrays = {k: np.ascontiguousarray(a) for k, a in arrays.items()}
    nc = bacc.Bacc("TRN2", target_bir_lowering=False, num_devices=1)
    io = {k: nc.dram_tensor(f"in_{k}", a.shape, F32, kind="ExternalInput").ap() for k, a in arrays.items()}
    io["out"] = nc.dram_tensor("out_0", (SEQS, T, D), F32, kind="ExternalOutput").ap()
    build(nc, io, at)
    r = run_bass_kernel_spmd(nc, [{f"in_{k}": a for k, a in arrays.items()}], core_ids=[0])
    return r.results[0]["out_0"]
```
